# Optimizing a Trainium2 kernel written in Bass

```python
import numpy as np
import jax
import jax.numpy as jnp

def _softmax(x, axis=-1):
    return jax.nn.softmax(x, axis=axis)

def _gelu(x):
    return jax.nn.gelu(x, approximate=True)

def _silu(x):
    return jax.nn.silu(x)

def _sigmoid(x):
    return jax.nn.sigmoid(x)

def _layernorm(x, axis=-1, eps=1e-05):
    m = jnp.mean(x, axis=axis, keepdims=True)
    v = jnp.var(x, axis=axis, keepdims=True)
    return (x - m) / jnp.sqrt(v + eps)

def _scatter_add(tgt, idx, src, axis=0):
    return tgt.at[idx].add(src)

def _segment_sum(src, seg, n):
    return jax.ops.segment_sum(src, seg, n)
kernel_name = 'mk_gnn_resnorm_d1_gnn_r32_e3c4f1'

def setup_inputs(seed: int=0):
    np.random.seed(seed)
    _w = jnp.asarray

    def _rec_inputs():
        import jax
        import jax.numpy as jnp
        _gk = jax.random.key(seed)
        x = -0.0003713 + 1 * jax.random.normal(jax.random.fold_in(_gk, 1), (50000, 256), jnp.float32)
        src = jax.random.randint(jax.random.fold_in(_gk, 2), (25000,), 0, 50000, jnp.int32)
        dst = jax.random.randint(jax.random.fold_in(_gk, 3), (25000,), 0, 50000, jnp.int32)
        _o = jnp.argsort(dst, stable=True)
        src = src[_o]
        dst = dst[_o]
        edge_type_8 = jax.random.randint(jax.random.fold_in(_gk, 12), (25000,), 0, 8, jnp.int32)
        return (x, src, dst, edge_type_8)
    x, src, dst, edge_type_8 = _rec_inputs()

    def _L0_gnn_setup():
        import jax, jax.numpy as jnp
        import numpy as np
        N_NODES = 50000
        N_EDGES = 25000
        D_IN = 256
        D_OUT = 256
        N_REL = 8
        key = jax.random.key(seed)
        k_x, k_ei, k_et, k_w = jax.random.split(key, 4)
        x = jax.random.normal(k_x, (N_NODES, D_IN), dtype=jnp.float32)
        edge_index = jax.random.randint(k_ei, (2, N_EDGES), 0, N_NODES, dtype=jnp.int32)
        edge_type = jax.random.randint(k_et, (N_EDGES,), 0, N_REL, dtype=jnp.int32)
        limit = float(np.sqrt(6.0 / (D_IN + D_OUT)))
        weight = jax.random.uniform(k_w, (N_REL, D_IN, D_OUT), dtype=jnp.float32, minval=-limit, maxval=limit)
        bias = jnp.zeros((D_OUT,), dtype=jnp.float32)
        return {'x': x, 'edge_index': edge_index, 'edge_type': edge_type, 'weight': weight, 'bias': bias}
    _L0_gnn_all = _L0_gnn_setup()
    _L0_gnn_in = {k: v for k, v in _L0_gnn_all.items() if k in ('weight', 'bias')}
    del _L0_gnn_all
    return {'x': x, 'src': src, 'dst': dst, 'edge_type_8': edge_type_8, 'L0_gnn_weight': _L0_gnn_in['weight'], 'L0_gnn_bias': _L0_gnn_in['bias']}

def reference(x, src, dst, edge_type_8, L0_gnn_weight, L0_gnn_bias):
    import jax
    import jax.numpy as jnp

    def _L0_gnn_ref(x, edge_index, edge_type, weight, bias):
        import jax, jax.numpy as jnp
        import numpy as np
        N_NODES = 50000
        N_EDGES = 25000
        D_IN = 256
        D_OUT = 256
        N_REL = 8
        num_nodes = x.shape[0]
        row, col = (edge_index[0], edge_index[1])
        xt = jnp.einsum('ni,rio->rno', x, weight)
        messages = xt[edge_type, col]
        out = jax.ops.segment_sum(messages, row, num_segments=num_nodes)
        return jax.nn.relu(out + bias)
    edge_index = jnp.stack([src, dst])
    x = _layernorm(x + _L0_gnn_ref(x, edge_index, edge_type_8, L0_gnn_weight, L0_gnn_bias), axis=-1)
    return x

_drawn_inputs = setup_inputs


def setup_inputs(seed=0):
    import zlib

    import numpy as np

    out = dict(_drawn_inputs(seed))
    spreads = {'L0_gnn_bias': (0.0, 0.1)}
    factors = {}
    for name, (base, spread) in spreads.items():
        noise = np.random.default_rng([zlib.crc32(name.encode()), seed]).standard_normal(out[name].shape)
        drawn = base * np.exp(spread * noise) if base else spread * noise
        out[name] = jnp.asarray(drawn.astype(out[name].dtype))
    for name, factor in factors.items():
        out[name] = (out[name] * factor).astype(out[name].dtype)
    return out
```

```python
from contextlib import ExitStack

import concourse.bass as bass
from concourse import mybir


P = 128
F32, BF16, FP16, I32, U32 = (mybir.dt.float32, mybir.dt.bfloat16, mybir.dt.float16, mybir.dt.int32, mybir.dt.uint32)
ALU = mybir.AluOpType
ACT = mybir.ActivationFunctionType
AX_X = mybir.AxisListType.X

N, D, E, R = 50000, 256, 25000, 8
KC = D // P
EP = 125
EC = E // EP
BUCKETS = -(-N // P)
PAIRS = -(-BUCKETS // 2)
LAST = N - (BUCKETS - 1) * P
SB = 4
SB_FIRST = [0, 98, 196, 294, 392]
SB_NEXT = max(b - a for a, b in zip(SB_FIRST, SB_FIRST[1:]))
GROUPS = SB * R
QUAD = 4
TILES_MAX = -(-(E // P + GROUPS + SB * (QUAD - 1)) // QUAD) * QUAD
QUADS_MAX = TILES_MAX // QUAD
HB, LB = 13, 32
WIN = 96
ROW = D + 8
assert SB == QUAD
GAP = P
ROWS = E + SB * GAP
RING = 7
ROUNDS = PAIRS // RING
SUM_BANK = [0, 1, 0, 1, 0, 1, 2]
assert PAIRS % RING == 0 and all(b % (2 * RING) == 0 for b in SB_FIRST)
WIDE = 64
NOWHERE = float(1 << 20)
EPS = 1e-5


def gnn_program(nc, x, src, dst, typ, weight, bias, out):
    with ExitStack() as ctx:
        def sb(name, shape, dt):
            return ctx.enter_context(nc.sbuf_tensor(name, shape, dt))

        def sem(name):
            return ctx.enter_context(nc.semaphore(name))

        messages = nc.dram_tensor("messages_dram", (ROWS, ROW), F32).ap()

        iota_bucket = sb("iota_bucket", [P, HB * LB], FP16)
        iota_node = sb("iota_node", [P, P], F32)
        neg_first = sb("neg_first", [P, 2 * PAIRS], F32)
        group_no = sb("group_no", [P, GROUPS], F32)
        before = sb("before", [P, P], BF16)
        upto = sb("upto", [P, P], BF16)
        before_f = sb("before_f", [P, HB], F32)
        ones = sb("ones", [P, P], BF16)
        ident = sb("ident", [P, P], F32)
        ones_f = sb("ones_f", [1, P], F32)
        zeros = sb("zeros", [P, 512], FP16)
        zero_rows = sb("zero_rows", [WIN, ROW], F32)
        src_i = sb("src_i", [EP, EC], I32)
        dst_i = sb("dst_i", [EP, EC], I32)
        typ_i = sb("typ_i", [EP, EC], I32)
        tmp_a = sb("tmp_a", [EP, EC], I32)
        tmp_b = sb("tmp_b", [EP, EC], I32)
        sblk = sb("sblk", [EP, EC], F32)
        key = sb("key", [EP, EC], FP16)
        planes = sb("planes", [EP, 3, EC], F32)
        bucket_hi = sb("bucket_hi", [EP, EC], F32)
        bucket_lo = sb("bucket_lo", [EP, EC], F32)
        in_group = sb("in_group", [EP, GROUPS, EC], BF16)
        counted = sb("counted", [EP, GROUPS, EC], F32)
        group_cnt = sb("group_cnt", [EP, GROUPS], BF16)
        group_tot = sb("group_tot", [P, GROUPS], I32)
        group_tiles = sb("group_tiles", [P, GROUPS], I32)
        tiles_upto = sb("tiles_upto", [P, GROUPS], F32)
        tiles_excl = sb("tiles_excl", [P, GROUPS], F32)
        sb_tiles = sb("sb_tiles", [P, SB], I32)
        sb_quads = sb("sb_quads", [P, SB], I32)
        sb_quads_f = sb("sb_quads_f", [P, SB], F32)
        sb_upto = sb("sb_upto", [P, SB], F32)
        sb_shift = sb("sb_shift", [P, SB], F32)
        quad_ends = sb("quad_ends", [P, SB + 1], I32)
        group_base = sb("group_base", [P, GROUPS], F32)
        group_off = sb("group_off", [P, GROUPS], F32)
        base_col = sb("base_col", [GROUPS, 1], F32)
        base_tmp = sb("base_tmp", [GROUPS, GROUPS], F32)
        col_weight = sb("col_weight", [GROUPS, 1], BF16)
        tile_cmp = sb("tile_cmp", [GROUPS, TILES_MAX], BF16)
        weight_off = sb("weight_off", [1, TILES_MAX], I32)
        slot_f = sb("slot_f", [EP, EC], F32)
        slot_i = sb("slot_i", [EP, EC], I32)
        slot_hi = sb("slot_hi", [EP, EC], F32)
        slot_lo = sb("slot_lo", [EP, EC], F32)
        put_lo = sb("put_lo", [EP, 4, 3, P], FP16)
        put_hi = sb("put_hi", [EP, 4, TILES_MAX], FP16)
        oh_hi = sb("oh_hi", [EP, EC, HB], BF16)
        oh_lo = sb("oh_lo", [EP, EC, LB], BF16)
        hist = sb("hist", [HB, LB], F32)
        hist_upto = sb("hist_upto", [HB, LB], F32)
        hist_start = sb("hist_start", [HB, LB], F32)
        row_start = sb("row_start", [P, HB * LB], F32)
        row_start_i = sb("row_start_i", [1, HB * LB], I32)
        got = sb("got", [P, 3, TILES_MAX], I32)
        tmp_c = sb("tmp_c", [P, TILES_MAX], I32)
        tmp_d = sb("tmp_d", [P, TILES_MAX], I32)
        dst_slot = sb("dst_slot", [P, TILES_MAX + QUAD], I32)
        src_slot = sb("src_slot", [P, TILES_MAX], F32)
        bucket_slot = sb("bucket_slot", [P, TILES_MAX], F32)
        skip_slot = sb("skip_slot", [P, TILES_MAX], F32)
        w_sb = sb("w_sb", [P, R * KC * D], F32)
        dst_quad = sb("dst_quad", [P, QUAD], U32)
        row_quad = sb("row_quad", [P, QUAD], U32)
        gathered = sb("gathered", [P, QUAD, D], F32)
        turned = sb("turned", [P, QUAD, KC, P], F32)
        msg = sb("msg", [P, QUAD, ROW], F32)
        in_bucket = sb("in_bucket", [P, QUAD, SB_NEXT], BF16)
        rank_prod = sb("rank_prod", [P, QUAD, SB_NEXT], F32)
        rank = sb("rank", [P, QUAD], F32)
        bias_in = sb("bias_in", [3, D], F32)
        bias_part = sb("bias_part", [3, 3, D], BF16)
        bias_rest = sb("bias_rest", [3, 2, D], F32)
        bias_sel = sb("bias_sel", [3, 3, D], F32)
        bias3 = sb("bias3", [3, 2, D], BF16)
        x_ring = sb("x_ring", [P, RING, 2, D], F32)
        win_ring = sb("win_ring", [WIN, RING, 2, ROW], F32)
        place = sb("place", [WIN, RING, 2, P], F32)
        z_ring = sb("z_ring", [P, RING, 2, D], F32)
        y_ring = sb("y_ring", [P, RING, 2, D], F32)
        stats = sb("stats", [P, RING, 2, 6], F32)
        mean_var = sb("mean_var", [P, RING, 2, 2], F32)
        std = sb("std", [P, RING, 2], F32)
        rstd = sb("rstd", [P, RING, 2], F32)
        shift = sb("shift", [P, RING, 2], F32)
        eps_col = sb("eps_col", [P, 1], F32)
        bucket_rows = sb("bucket_rows", [1, BUCKETS], I32)
        bucket_wins = sb("bucket_wins", [1, BUCKETS], I32)
        bucket_wins_f = sb("bucket_wins_f", [1, BUCKETS], F32)
        win_ends = sb("win_ends", [1, BUCKETS + 1], I32)
        most_rows = sb("most_rows", [1, 1], F32)
        crowded = sb("crowded", [1, 1], I32)

        bank = [ctx.enter_context(nc.psum_tensor(f"bank{i}", [P, 512], F32)) for i in range(8)]

        edges_in, weights_in, bias_loaded = sem("edges_in"), sem("weights_in"), sem("bias_loaded")
        consts, consts_step = sem("consts"), sem("consts_step")
        dve_step, settled = sem("dve_step"), sem("settled")
        cnt_ready, tots_ready, base_ready, tile_cmp_ready, relation_ready = (
            sem("cnt_ready"), sem("tots_ready"), sem("base_ready"), sem("tile_cmp_ready"), sem("relation_ready"))
        onehots_ready, hist_ready, hist_copied, hist_prefixed, starts_ready, rowstart_psum = (
            sem("onehots_ready"), sem("hist_ready"), sem("hist_copied"), sem("hist_prefixed"), sem("starts_ready"),
            sem("rowstart_psum"))
        tables_ready, windows_ready = sem("tables_ready"), sem("windows_ready")
        put_ready, put_used, put_done = sem("put_ready"), sem("put_used"), sem("put_done")
        slots_ready = sem("slots_ready")
        gather_done = [sem(f"gather_done{u}") for u in range(QUAD)]
        scatter_done = [sem(f"scatter_done{u}") for u in range(QUAD)]
        dst_ready, turned_psum, turned_ready, msg_psum, msg_ready, src_put = (
            sem("dst_ready"), sem("turned_psum"), sem("turned_ready"), sem("msg_psum"), sem("msg_ready"),
            sem("src_put"))
        
        bucket_ready, rank_psum, rank_read, rank_used, row_ready, rank_step = (
            sem("bucket_ready"), sem("rank_psum"), sem("rank_read"), sem("rank_used"), sem("row_ready"),
            sem("rank_step"))
        x_in = [sem(f"x_in{s}") for s in range(RING)]
        win_in = [sem(f"win_in{s}") for s in range(RING)]
        y_out = [sem(f"y_out{s}") for s in range(RING)]
        bias_ready, place_ready, sum_psum, z_ready, stats_ready, rstd_ready, mv_ready, std_ready, norm_ready, y_ready = (
            sem("bias_ready"), sem("place_ready"), sem("sum_psum"), sem("z_ready"), sem("stats_ready"), sem("rstd_ready"),
            sem("mv_ready"), sem("std_ready"), sem("norm_ready"), sem("y_ready"))

        x_again, rows_again, y_again = sem("x_again"), sem("rows_again"), sem("y_again")
        place_again, summed_again, z_again, dve_again, norm_again, std_again, done_again = (
            sem("place_again"), sem("summed_again"), sem("z_again"), sem("dve_again"), sem("norm_again"), sem("std_again"),
            sem("done_again"))

        put_bank = bank[0:3]
        hist_bank, row_bank, small_bank = bank[3], bank[4], bank[5]
        turned_bank, msg_bank, rank_bank, sum_bank = bank[0:2], bank[2:4], bank[4], bank[5:8]

        def slot_before(it, s, back):
            return (it, s - back) if s >= back else (it - 1, s - back + RING)

        def settle(eng):
            eng.sem_inc(settled, 1)

        def superblock_quads(eng, g):
            first = 0 if g == 0 else eng.value_load(quad_ends[0:1, g:g + 1], min_val=g, max_val=QUADS_MAX - 1)
            end = eng.value_load(quad_ends[0:1, g + 1:g + 2], min_val=g + 1, max_val=QUADS_MAX)
            return first, end

        def again(eng, body):
            def one(b, nodes):
                w0 = 0 if isinstance(b, int) and b == 0 else eng.value_load(
                    win_ends[0:1, bass.ds(b, 1)], min_val=0, max_val=BUCKETS + E // WIDE)
                w1 = eng.value_load(win_ends[0:1, bass.ds(b + 1, 1)], min_val=1, max_val=BUCKETS + E // WIDE + 1)
                body(b, nodes, w0, w1)

            eng.wait_ge(windows_ready, 1)
            with eng.If(eng.value_load(crowded[0:1, 0:1], min_val=0, max_val=1)):
                with eng.Fori(0, BUCKETS - 1) as b:
                    one(b, P)
                one(BUCKETS - 1, LAST)

        block = ctx.enter_context(nc.Block())

        @block.sync
        def _(sp):
            sp.dma_start(src_i[:, :], src).then_inc(edges_in, 16)
            sp.dma_start(dst_i[:, :], dst).then_inc(edges_in, 16)
            sp.dma_start(typ_i[:, :], typ).then_inc(edges_in, 16)
            sp.dma_start(bias_in[:, :], bias.to_broadcast([3, D])).then_inc(bias_loaded, 16)
            for r in range(R):
                sp.dma_start(w_sb[:, r * KC * D:(r + 1) * KC * D].rearrange("p (k o) -> p k o", k=KC),
                             weight[r].rearrange("(k p) o -> p k o", p=P)).then_inc(weights_in, 16)
            sp.wait_ge(tables_ready, 1)

            def load_pair(it, s, nodes):
                i = it * RING + s
                if not isinstance(it, int) or it > 0:
                    sp.wait_ge(z_ready, i - RING + 1)
                    settle(sp)
                if nodes == 2 * P:
                    sp.dma_start(x_ring[:, s, :, :], x[bass.ds(i * (2 * P), 2 * P), :].rearrange(
                        "(u p) d -> p u d", p=P)).then_inc(x_in[s], 16)
                else:
                    sp.dma_start(x_ring[0:nodes, s, 0, :], x[i * 2 * P:i * 2 * P + nodes, :]).then_inc(x_in[s], 16)
                for u in range(2 if nodes == 2 * P else 1):
                    at = sp.value_load(row_start_i[0:1, bass.ds(i * 2 + u, 1)], min_val=0, max_val=ROWS - WIN)
                    sp.dma_start(win_ring[:, s, u, :], messages[bass.ds(at, WIN), :]).then_inc(win_in[s], 16)

            for g in range(SB):
                _, end = superblock_quads(sp, g)
                for u in range(QUAD):
                    sp.wait_ge(scatter_done[u], end * 16 + 16)
                settle(sp)
                first, last = SB_FIRST[g] // 2 // RING, SB_FIRST[g + 1] // 2 // RING
                if g == 0:
                    for s in range(RING):
                        load_pair(0, s, 2 * P)
                    first = 1
                if g == SB - 1:
                    last -= 1
                with sp.Fori(first, last) as it:
                    for s in range(RING):
                        load_pair(it, s, 2 * P)
            for s in range(RING):
                load_pair(ROUNDS - 1, s, 2 * P if s < RING - 1 else LAST)

            sp.wait_ge(z_ready, PAIRS)

            def load_again(b, nodes, w0, w1):
                sp.wait_ge(z_again, b + 1)
                settle(sp)
                sp.dma_start(x_ring[0:nodes, 0, 0, :], x[bass.ds(b * P, nodes), :]).then_inc(x_again, 16)
                at = sp.value_load(row_start_i[0:1, bass.ds(b, 1)], min_val=0, max_val=E + GAP * (SB - 1))
                with sp.Fori(w0, w1) as w:
                    sp.wait_ge(summed_again, w + 1)
                    settle(sp)
                    first = nc.s_assert_within(at + (w - w0) * WIDE, 0, ROWS - WIDE)
                    sp.dma_start(win_ring[0:WIDE, 0, 0, :], messages[bass.ds(first, WIDE), :]
                                 ).then_inc(rows_again, 16)

            again(sp, load_again)

        @block.gpsimd
        def _(pool):
            pool.memset(ones[:, :], 1.0)
            pool.memset(ones_f[:, :], 1.0)
            pool.memset(before[:, :], 1.0)
            pool.memset(upto[:, :], 1.0)
            pool.memset(before_f[:, :], 1.0)
            pool.memset(zeros[:, :], 0.0)
            pool.memset(zero_rows[:, :], 0.0)
            pool.memset(eps_col[:, :], EPS)
            pool.memset(quad_ends[:, :], 0)
            pool.memset(win_ends[:, :], 0)
            pool.memset(dst_slot[:, TILES_MAX:TILES_MAX + QUAD], 0)
            pool.memset(ident[:, :], 0.0).then_inc(consts_step, 1)
            pool.memset(msg[:, :, :], 0.0)
            pool.iota(iota_bucket[:, :], pattern=[[1, HB * LB]], base=0, channel_multiplier=0,
                      allow_small_or_imprecise_dtypes=True)
            pool.iota(iota_node[:, :], pattern=[[1, P]], base=0, channel_multiplier=0,
                      allow_small_or_imprecise_dtypes=True)
            pool.iota(neg_first[:, :], pattern=[[-P, 2 * PAIRS]], base=0, channel_multiplier=0,
                      allow_small_or_imprecise_dtypes=True)
            pool.iota(group_no[:, :], pattern=[[1, GROUPS]], base=0, channel_multiplier=0,
                      allow_small_or_imprecise_dtypes=True)
            pool.wait_ge(consts_step, 1)
            pool.affine_select(out=before[:, :], in_=before[:, :], compare_op=ALU.is_gt, fill=0.0, base=0,
                               pattern=[[1, P]], channel_multiplier=-1)
            pool.affine_select(out=before_f[:, :], in_=before_f[:, :], compare_op=ALU.is_gt, fill=0.0, base=0,
                               pattern=[[1, HB]], channel_multiplier=-1)
            pool.affine_select(out=upto[:, :], in_=upto[:, :], compare_op=ALU.is_ge, fill=0.0, base=0,
                               pattern=[[-1, P]], channel_multiplier=1)
            pool.affine_select(out=ident[:, :], in_=ident[:, :], compare_op=ALU.not_equal, fill=1.0, base=0,
                               pattern=[[-1, P]], channel_multiplier=1).then_inc(consts, 1)

            def gather(u):
                pool.indirect_dma_start(gathered[:, u, :], None, x, bass.IndirectOffsetOnAxis(dst_quad[:, u:u + 1], 0)
                                        ).then_inc(gather_done[u], 16)

            def scatter(u):
                pool.indirect_dma_start(messages, bass.IndirectOffsetOnAxis(row_quad[:, u:u + 1], 0), msg[:, u, :],
                                        None, bounds_check=ROWS - 1, oob_is_err=False).then_inc(scatter_done[u], 16)

            pool.wait_ge(consts, 1)
            pool.wait_ge(tables_ready, 1)
            for g in range(SB):
                end = pool.value_load(row_start_i[0:1, SB_FIRST[g + 1]:SB_FIRST[g + 1] + 1],
                                      min_val=GAP * (g + 1), max_val=E + GAP * (g + 1))
                pool.dma_start(messages[bass.ds(end - GAP, WIN), :], zero_rows[:, :]).then_inc(scatter_done[g], 16)

            pool.wait_ge(dst_ready, 1)
            for u in range(QUAD):
                gather(u)
            quads = pool.value_load(quad_ends[0:1, SB:SB + 1], min_val=SB, max_val=QUADS_MAX)
            with pool.Fori(1, quads) as q:
                pool.wait_ge(dst_ready, q + 1)
                pool.wait_ge(turned_psum, q * 2)
                settle(pool)
                for u in range(QUAD):
                    gather(u)
                pool.wait_ge(row_ready, q)
                pool.wait_ge(src_put, q)
                for u in range(QUAD):
                    if u % 2 == 0:
                        pool.wait_ge(msg_ready, q * 2 + u // 2 + 1)
                        settle(pool)
                    scatter(u)
            pool.wait_ge(row_ready, quads)
            pool.wait_ge(src_put, quads)
            pool.wait_ge(msg_ready, quads * 2 + 2)
            settle(pool)
            for u in range(QUAD):
                scatter(u)

        @block.scalar
        def _(act):
            act.sem_inc(msg_ready, 2)
            act.wait_ge(tables_ready, 1)
            act.wait_ge(slots_ready, 1)
            quads = act.value_load(quad_ends[0:1, SB:SB + 1], min_val=SB, max_val=QUADS_MAX)

            def next_dst(q):
                nc.scalar.copy(dst_quad[:, :], dst_slot[:, bass.ds(q * QUAD, QUAD)]).then_inc(dst_ready, 1)

            next_dst(0)
            with act.Fori(0, quads) as q:
                for h in range(2):
                    act.wait_ge(turned_psum, q * 2 + h + 1)
                    act.wait_ge(msg_psum, q * 2 + h + 1)
                    nc.scalar.copy(turned[:, 2 * h:2 * h + 2, :, :].rearrange("p a b c -> p (a b c)"),
                                   turned_bank[h][:, :]).then_inc(turned_ready, 1)
                for u in range(QUAD):
                    act.wait_ge(gather_done[u], q * 16 + 16)
                nc.scalar.copy(dst_quad[:, :], dst_slot[:, bass.ds((q + 1) * QUAD, QUAD)]).then_inc(dst_ready, 1)
                for h in range(2):
                    act.wait_ge(msg_psum, q * 2 + h + 3)
                    for u in (2 * h, 2 * h + 1):
                        act.wait_ge(scatter_done[u], q * 16 + 16)
                    nc.scalar.copy(msg[:, 2 * h:2 * h + 2, 0:D],
                                   msg_bank[h][:, :].rearrange("p (u d) -> p u d", u=2)).then_inc(msg_ready, 1)

            def root(it, s):
                act.wait_ge(mv_ready, it * RING + s + 1)
                nc.scalar.activation(std[:, s, :], mean_var[:, s, :, 1], ACT.Sqrt, bias=eps_col[:, 0:1]
                                     ).then_inc(std_ready, 1)

            def normalize(it, s, nodes):
                act.wait_ge(norm_ready, it * RING + s + 1)
                if not isinstance(it, int) or it > 0:
                    act.wait_ge(y_out[s], it * 16)
                rows = P if nodes == 2 * P else nodes
                for u in range(2 if nodes == 2 * P else 1):
                    last = nc.scalar.activation(y_ring[0:rows, s, u, :], z_ring[0:rows, s, u, :], ACT.Identity,
                                                scale=rstd[0:rows, s, u:u + 1], bias=shift[0:rows, s, u:u + 1])
                last.then_inc(y_ready, 1)

            def store(it, s, nodes):
                i = it * RING + s
                act.wait_ge(y_ready, i + 1)
                if nodes == 2 * P:
                    act.dma_start(out[bass.ds(i * (2 * P), 2 * P), :].rearrange("(u p) d -> p u d", p=P),
                                  y_ring[:, s, :, :]).then_inc(y_out[s], 16)
                else:
                    act.dma_start(out[i * 2 * P:i * 2 * P + nodes, :], y_ring[0:nodes, s, 0, :]
                                  ).then_inc(y_out[s], 16)

            def act_step(it, s, fills):
                root(it, s)
                if fills or s >= 1:
                    normalize(*slot_before(it, s, 1), 2 * P)
                if fills or s >= 2:
                    store(*slot_before(it, s, 2), 2 * P)

            for s in range(RING):
                act_step(0, s, False)
            with act.Fori(1, ROUNDS) as it:
                for s in range(RING):
                    act_step(it, s, True)
            store(ROUNDS - 1, RING - 2, 2 * P)
            normalize(ROUNDS - 1, RING - 1, LAST)
            store(ROUNDS - 1, RING - 1, LAST)
            for s in range(RING):
                act.wait_ge(y_out[s], 16 * ROUNDS)

            act.sem_inc(y_again, 1)

            def finish_again(b, nodes, w0, w1):
                act.wait_ge(norm_again, b * 2 + 1)
                nc.scalar.activation(std[:, 0, 0:1], mean_var[:, 0, 0, 1:2], ACT.Sqrt, bias=eps_col[:, 0:1]
                                     ).then_inc(std_again, 1)
                act.wait_ge(norm_again, b * 2 + 2)
                nc.scalar.activation(y_ring[0:nodes, 0, 0, :], z_ring[0:nodes, 0, 0, :], ACT.Identity,
                                     scale=rstd[0:nodes, 0, 0:1], bias=shift[0:nodes, 0, 0:1]).then_inc(y_again, 1)
                act.wait_ge(y_again, b + 2)
                act.dma_start(out[bass.ds(b * P, nodes), :], y_ring[0:nodes, 0, 0, :]).then_inc(done_again, 16)
                act.wait_ge(done_again, b * 16 + 16)

            again(act, finish_again)

        @block.tensor
        def _(pe):
            pe.sem_inc(put_used, 4)
            pe.sem_inc(msg_psum, 2)
            pe.sem_inc(rank_used, 1)
            pe.wait_ge(consts, 1)
            pe.wait_ge(cnt_ready, 1)
            nc.tensor.matmul(small_bank[0:EP, 0:GROUPS], before[0:EP, 0:EP], group_cnt[:, :], start=True, stop=True)
            nc.tensor.matmul(small_bank[:, 64:64 + GROUPS], ones[0:EP, :], group_cnt[:, :], start=True, stop=True
                             ).then_inc(tots_ready, 1)
            for v in range(3):
                nc.tensor.matmul(put_bank[v][:, 0:TILES_MAX], zeros[0:1, 0:P], zeros[0:1, 0:TILES_MAX],
                                 start=True, stop=False, skip_group_check=True)
            with pe.Fori(0, EC // 4) as it:
                for c in range(4):
                    pe.wait_ge(put_ready, it * 4 + c + 1)
                    for v in range(3):
                        last = nc.tensor.matmul(put_bank[v][:, 0:TILES_MAX], put_lo[:, c, v, :], put_hi[:, c, :],
                                                start=False, stop=False, skip_group_check=True)
                    last.then_inc(put_used, 1)
            for v in range(3):
                last = nc.tensor.matmul(put_bank[v][:, 0:TILES_MAX], zeros[0:1, 0:P], zeros[0:1, 0:TILES_MAX],
                                        start=False, stop=True, skip_group_check=True)
            last.then_inc(put_done, 1)

            pe.wait_ge(tile_cmp_ready, 1)
            nc.tensor.matmul(small_bank[0:1, 128:128 + TILES_MAX], col_weight[:, :], tile_cmp[:, :], start=True,
                             stop=True).then_inc(relation_ready, 1)
            pe.wait_ge(onehots_ready, 1)
            nc.tensor.matmul(hist_bank[0:HB, 0:LB], oh_hi[:, 0, :], oh_lo[:, 0, :], start=True, stop=False)
            for c in range(1, EC):
                last = nc.tensor.matmul(hist_bank[0:HB, 0:LB], oh_hi[:, c, :], oh_lo[:, c, :],
                                        start=False, stop=(c == EC - 1))
            last.then_inc(hist_ready, 1)
            pe.wait_ge(hist_prefixed, 1)
            nc.tensor.matmul(hist_bank[0:HB, 64:65], before_f[0:HB, 0:HB], hist_upto[:, LB - 1:LB],
                             start=True, stop=True).then_inc(hist_copied, 1)
            pe.wait_ge(starts_ready, 1)
            for h in range(HB):
                last = nc.tensor.matmul(row_bank[:, h * LB:(h + 1) * LB], ident[0:HB, h:h + 1].to_broadcast([HB, P]),
                                        hist_start[:, :], start=True, stop=True)
            last.then_inc(rowstart_psum, 1)

            pe.wait_ge(tables_ready, 1)
            pe.wait_ge(slots_ready, 1)
            pe.wait_ge(weights_in, 16 * R)
            rank_v = rank_bank[:, 0:QUAD * SB_NEXT].rearrange("p (u b) -> p u b", u=QUAD)

            def count(lhs, tile, to, n):
                return nc.tensor.matmul(rank_v[:, to:to + n, :], lhs,
                                        in_bucket[:, tile:tile + 1, :].to_broadcast([P, n, SB_NEXT]),
                                        start=False, stop=False, skip_group_check=True)

            for g in range(SB):
                first, end = superblock_quads(pe, g)
                if g > 0:
                    pe.wait_ge(rank_read, first)
                nc.tensor.matmul(rank_v[:, :, :], ones_f[0:1, :],
                                 row_start[0:1, SB_FIRST[g]:SB_FIRST[g] + SB_NEXT].rearrange(
                                     "p (u b) -> p u b", u=1).to_broadcast([1, QUAD, SB_NEXT]),
                                 start=True, stop=False, skip_group_check=True)
                with pe.Fori(first, end) as q:
                    pe.wait_ge(bucket_ready, q + 1)
                    for u in range(QUAD):
                        last = count(before[:, :], u, u, 1)
                        if u < QUAD - 1:
                            last = count(ones[:, :], u, u + 1, QUAD - 1 - u)
                    last.then_inc(rank_psum, 1)
                    for h in range(2):
                        for u in (2 * h, 2 * h + 1):
                            pe.wait_ge(gather_done[u], q * 16 + 16)
                        for u in (2 * h, 2 * h + 1):
                            for k in range(KC):
                                last = nc.tensor.transpose(
                                    turned_bank[h][:, ((u - 2 * h) * KC + k) * P:((u - 2 * h) * KC + k + 1) * P],
                                    gathered[:, u, k * P:(k + 1) * P], ident[:, :])
                        last.then_inc(turned_psum, 1)
                    for h in range(2):
                        pe.wait_ge(turned_ready, q * 2 + h + 1)
                        pe.wait_ge(msg_ready, q * 2 + h + 1)
                        for u in (2 * h, 2 * h + 1):
                            at = pe.value_load(weight_off[0:1, bass.ds(q * QUAD + u, 1)], min_val=0,
                                               max_val=(R - 1) * KC * D)
                            for k in range(KC):
                                last = nc.tensor.matmul(msg_bank[h][:, (u - 2 * h) * D:(u - 2 * h + 1) * D],
                                                        turned[:, u, k, :], w_sb[:, bass.ds(at + k * D, D)],
                                                        start=(k == 0), stop=(k == KC - 1), skip_group_check=True)
                        last.then_inc(msg_psum, 1)
                    pe.wait_ge(rank_read, q + 1)
                    for u in range(QUAD):
                        if u > 0:
                            count(ones[:, :], u, 0, u)
                        last = count(upto[:, :], u, u, 1)
                    last.then_inc(rank_used, 1)

            pe.wait_ge(bias_ready, 1)

            def sum_pair(it, s, nodes):
                to = sum_bank[SUM_BANK[s]]
                if not isinstance(it, int) or it > 0 or s >= 2:
                    pe.wait_ge(z_ready, it * RING + s - 1)
                nc.tensor.matmul(to[:, :], ones[0:3, :], bias3[:, :, :].rearrange("p u d -> p (u d)"),
                                 start=True, stop=False, skip_group_check=True)
                pe.wait_ge(place_ready, it * RING + s + 1)
                for u in range(2 if nodes == 2 * P else 1):
                    last = nc.tensor.matmul(to[:, u * D:(u + 1) * D], place[:, s, u, :],
                                            win_ring[:, s, u, 0:D], start=False, stop=True, skip_group_check=True)
                last.then_inc(sum_psum, 1)

            for s in range(RING):
                sum_pair(0, s, 2 * P)
            with pe.Fori(1, ROUNDS - 1) as it:
                for s in range(RING):
                    sum_pair(it, s, 2 * P)
            for s in range(RING):
                sum_pair(ROUNDS - 1, s, 2 * P if s < RING - 1 else LAST)

            pe.wait_ge(z_ready, PAIRS)
            pe.sem_inc(summed_again, 1)

            def sum_again(b, nodes, w0, w1):
                pe.wait_ge(z_again, b + 1)
                nc.tensor.matmul(sum_bank[0][:, 0:D], ones[0:3, :], bias3[:, 0, :], start=True, stop=False,
                                 skip_group_check=True)
                with pe.Fori(w0, w1) as w:
                    pe.wait_ge(place_again, w + 1)
                    nc.tensor.matmul(sum_bank[0][:, 0:D], place[0:WIDE, 0, 0, :], win_ring[0:WIDE, 0, 0, 0:D],
                                     start=False, stop=True, skip_group_check=True).then_inc(summed_again, 1)

            again(pe, sum_again)

        @block.vector
        def _(dve):
            steps = [0]

            def step(ins):
                steps[0] += 1
                ins.then_inc(dve_step, 1)
                dve.wait_ge(dve_step, steps[0])

            dve.wait_ge(edges_in, 48)
            dve.wait_ge(consts, 1)
            step(nc.vector.tensor_scalar(sblk[:, :], src_i[:, :], float(SB_FIRST[1] * P), None, ALU.is_ge))
            for g in range(2, SB):
                step(nc.vector.scalar_tensor_tensor(sblk[:, :], src_i[:, :], float(SB_FIRST[g] * P), sblk[:, :],
                                                    ALU.is_ge, ALU.add))
            step(nc.vector.scalar_tensor_tensor(key[:, :], sblk[:, :], float(R), typ_i[:, :], ALU.mult, ALU.add))
            for k in range(GROUPS):
                last = nc.vector.tensor_scalar(in_group[:, k, :], key[:, :], float(k), None, ALU.is_equal)
            step(last)
            for k in range(GROUPS):
                last = nc.vector.tensor_tensor_scan(counted[:, k, :], zeros[0:EP, 0:EC], in_group[:, k, :], 0.0,
                                                    ALU.add, ALU.add)
            step(last)
            nc.vector.tensor_copy(group_cnt[:, :], counted[:, :, EC - 1]).then_inc(cnt_ready, 1)
            nc.vector.tensor_scalar(tmp_a[:, :], dst_i[:, :], 31, 5, ALU.bitwise_and, ALU.logical_shift_left)
            step(nc.vector.tensor_scalar(tmp_b[:, :], src_i[:, :], 31, None, ALU.bitwise_and))
            nc.vector.scalar_tensor_tensor(planes[:, 2, :], tmp_a[:, :], 1024.0, tmp_b[:, :], ALU.add, ALU.add)
            step(nc.vector.tensor_scalar(slot_i[:, :], dst_i[:, :], 5, None, ALU.logical_shift_right))
            step(nc.vector.tensor_copy(planes[:, 0, :], slot_i[:, :]))
            step(nc.vector.tensor_scalar(slot_i[:, :], src_i[:, :], 5, None, ALU.logical_shift_right))
            step(nc.vector.tensor_copy(planes[:, 1, :], slot_i[:, :]))
            step(nc.vector.tensor_scalar(tmp_a[:, :], src_i[:, :], 12, None, ALU.logical_shift_right))
            step(nc.vector.tensor_scalar(tmp_b[:, :], src_i[:, :], 7, LB - 1, ALU.logical_shift_right,
                                         ALU.bitwise_and))
            nc.vector.tensor_copy(bucket_hi[:, :], tmp_a[:, :])
            step(nc.vector.tensor_copy(bucket_lo[:, :], tmp_b[:, :]))

            dve.wait_ge(tots_ready, 1)
            step(nc.vector.tensor_scalar(group_tot[:, :], small_bank[:, 64:64 + GROUPS], float(P - 1), None, ALU.add))
            step(nc.vector.tensor_scalar(group_tiles[:, :], group_tot[:, :], 7, None, ALU.logical_shift_right))
            step(nc.vector.tensor_tensor_scan(tiles_upto[:, :], zeros[:, 0:GROUPS], group_tiles[:, :], 0.0,
                                              ALU.add, ALU.add))
            step(nc.vector.tensor_tensor(tiles_excl[:, :], tiles_upto[:, :], group_tiles[:, :], ALU.subtract))
            upto_v = tiles_upto[:, :].rearrange("p (g r) -> p g r", g=SB)
            excl_v = tiles_excl[:, :].rearrange("p (g r) -> p g r", g=SB)
            step(nc.vector.scalar_tensor_tensor(sb_tiles[:, :], upto_v[:, :, R - 1], float(QUAD - 1),
                                                excl_v[:, :, 0], ALU.add, ALU.subtract))
            step(nc.vector.tensor_scalar(sb_quads[:, :], sb_tiles[:, :], 2, None, ALU.logical_shift_right))
            step(nc.vector.tensor_scalar(sb_quads_f[:, :], sb_quads[:, :], 1.0, None, ALU.max))
            step(nc.vector.tensor_tensor_scan(sb_upto[:, :], zeros[:, 0:SB], sb_quads_f[:, :], 0.0,
                                              ALU.add, ALU.add))
            nc.vector.tensor_copy(quad_ends[:, 1:SB + 1], sb_upto[:, :])
            step(nc.vector.tensor_tensor(sb_quads_f[:, :], sb_upto[:, :], sb_quads_f[:, :], ALU.subtract))
            step(nc.vector.scalar_tensor_tensor(sb_shift[:, :], sb_quads_f[:, :], float(QUAD), excl_v[:, :, 0],
                                                ALU.mult, ALU.subtract))
            step(nc.vector.tensor_tensor(group_base[:, :].rearrange("p (g r) -> p g r", g=SB), excl_v,
                                         sb_shift[:, :].rearrange("p (g r) -> p g r", r=1).to_broadcast([P, SB, R]),
                                         ALU.add))
            step(nc.vector.tensor_scalar(group_off[:, :], group_base[:, :], float(P), -1.0, ALU.mult, ALU.add))
            step(nc.vector.tensor_tensor(group_off[0:EP, :], group_off[0:EP, :], small_bank[0:EP, 0:GROUPS],
                                         ALU.add))
            for k in range(GROUPS):
                last = nc.vector.scalar_tensor_tensor(counted[:, k, :], counted[:, k, :], group_off[0:EP, k:k + 1],
                                                      in_group[:, k, :], ALU.add, ALU.mult)
            step(last)
            step(nc.vector.tensor_reduce(slot_f[:, :], counted[:, :, :].rearrange("p k c -> p c k"), AX_X, ALU.add))
            step(nc.vector.tensor_copy(slot_i[:, :], slot_f[:, :]))
            nc.vector.tensor_scalar(tmp_a[:, :], slot_i[:, :], 7, None, ALU.logical_shift_right)
            step(nc.vector.tensor_scalar(tmp_b[:, :], slot_i[:, :], P - 1, None, ALU.bitwise_and))
            nc.vector.tensor_copy(slot_hi[:, :], tmp_a[:, :])
            step(nc.vector.tensor_copy(slot_lo[:, :], tmp_b[:, :]))

            with dve.Fori(0, EC // 4) as it:
                for c in range(4):
                    dve.wait_ge(put_used, it * 4 + c + 1)
                    for v in range(3):
                        nc.vector.tensor_scalar(put_lo[:, c, v, :], iota_bucket[0:EP, 0:P],
                                                slot_lo[:, bass.ds(it * 4 + c, 1)],
                                                planes[:, v, bass.ds(it * 4 + c, 1)], ALU.is_equal, ALU.mult)
                    nc.vector.tensor_scalar(put_hi[:, c, :], iota_bucket[0:EP, 0:TILES_MAX],
                                            slot_hi[:, bass.ds(it * 4 + c, 1)], None, ALU.is_equal
                                            ).then_inc(put_ready, 1)

            step(nc.vector.tensor_tensor_reduce(base_tmp[:, :], group_base[0:GROUPS, :], ident[0:GROUPS, 0:GROUPS],
                                                1.0, 0.0, ALU.mult, ALU.add, base_col[:, :]))
            nc.vector.tensor_scalar(tile_cmp[:, :], iota_bucket[0:GROUPS, 0:TILES_MAX], base_col[:, 0:1], None,
                                    ALU.is_ge)
            step(nc.vector.tensor_reduce(base_tmp[:, 0:1], ident[0:GROUPS, 0:GROUPS].rearrange(
                "p (g r) -> p r g", r=R)[:, 0, :], AX_X, ALU.add))
            step(nc.vector.tensor_scalar(base_tmp[:, 1:2], base_tmp[:, 0:1], -float(R), 1.0, ALU.mult, ALU.add))
            nc.vector.scalar_tensor_tensor(col_weight[:, :], ident[0:GROUPS, 0:1], float(R - 1), base_tmp[:, 1:2],
                                           ALU.mult, ALU.add).then_inc(tile_cmp_ready, 1)
            dve.wait_ge(relation_ready, 1)
            step(nc.vector.tensor_scalar(weight_off[:, :], small_bank[0:1, 128:128 + TILES_MAX], float(KC * D), None,
                                         ALU.mult))

            nc.vector.tensor_tensor(oh_hi[:, :, :],
                                    iota_bucket[0:EP, 0:HB].rearrange("p (c h) -> p c h", c=1).to_broadcast(
                                        [EP, EC, HB]),
                                    bucket_hi[:, :].rearrange("p (c h) -> p c h", h=1).to_broadcast([EP, EC, HB]),
                                    ALU.is_equal)
            nc.vector.tensor_tensor(oh_lo[:, :, :],
                                    iota_bucket[0:EP, 0:LB].rearrange("p (c h) -> p c h", c=1).to_broadcast(
                                        [EP, EC, LB]),
                                    bucket_lo[:, :].rearrange("p (c h) -> p c h", h=1).to_broadcast([EP, EC, LB]),
                                    ALU.is_equal).then_inc(onehots_ready, 1)
            dve.wait_ge(hist_ready, 1)
            step(nc.vector.tensor_copy(hist[:, :], hist_bank[0:HB, 0:LB]))
            nc.vector.tensor_tensor_scan(hist_upto[:, :], zeros[0:HB, 0:LB], hist[:, :], 0.0, ALU.add, ALU.add
                                         ).then_inc(hist_prefixed, 1)
            dve.wait_ge(hist_copied, 1)
            step(nc.vector.tensor_tensor(hist_start[:, :], hist_upto[:, :], hist[:, :], ALU.subtract))
            nc.vector.tensor_scalar(hist_start[:, :], hist_start[:, :], hist_bank[0:HB, 64:65], None, ALU.add
                                    ).then_inc(starts_ready, 1)
            dve.wait_ge(rowstart_psum, 1)
            for g in range(SB + 1):
                a, b = SB_FIRST[g], (SB_FIRST[g + 1] if g < SB else HB * LB)
                last = nc.vector.tensor_scalar(row_start[:, a:b], row_bank[:, a:b], float(g * GAP), None, ALU.add)
            step(last)
            step(nc.vector.tensor_copy(row_start_i[:, :], row_start[0:1, :]))
            nc.vector.tensor_tensor(bucket_rows[:, :], row_start[0:1, 1:BUCKETS + 1], row_start[0:1, 0:BUCKETS],
                                    ALU.subtract).then_inc(tables_ready, 1)

            dve.wait_ge(put_done, 1)
            for v in range(3):
                last = nc.vector.tensor_copy(got[:, v, :], put_bank[v][:, 0:TILES_MAX])
            step(last)
            step(nc.vector.tensor_scalar(tmp_c[:, :], got[:, 0, :], 5, None, ALU.logical_shift_left))
            step(nc.vector.tensor_scalar(tmp_d[:, :], got[:, 2, :], 5, 31, ALU.logical_shift_right, ALU.bitwise_and))
            step(nc.vector.tensor_tensor(dst_slot[:, 0:TILES_MAX], tmp_c[:, :], tmp_d[:, :], ALU.add))
            step(nc.vector.tensor_scalar(tmp_c[:, :], got[:, 2, :], 31, None, ALU.bitwise_and))
            step(nc.vector.scalar_tensor_tensor(src_slot[:, :], got[:, 1, :], 32.0, tmp_c[:, :], ALU.mult, ALU.add))
            step(nc.vector.tensor_scalar(skip_slot[:, :], got[:, 2, :], 1024.0, NOWHERE, ALU.is_lt, ALU.mult))
            step(nc.vector.tensor_scalar(tmp_d[:, :], got[:, 1, :], 2, None, ALU.logical_shift_right))
            step(nc.vector.tensor_tensor(bucket_slot[:, :], tmp_d[:, :], skip_slot[:, :], ALU.add))
            dve.sem_inc(slots_ready, 1)

            dve.wait_ge(bias_loaded, 16)
            step(nc.vector.tensor_copy(bias_part[:, 0, :], bias_in[:, :]))
            step(nc.vector.tensor_tensor(bias_rest[:, 0, :], bias_in[:, :], bias_part[:, 0, :], ALU.subtract))
            step(nc.vector.tensor_copy(bias_part[:, 1, :], bias_rest[:, 0, :]))
            step(nc.vector.tensor_tensor(bias_rest[:, 1, :], bias_rest[:, 0, :], bias_part[:, 1, :], ALU.subtract))
            step(nc.vector.tensor_copy(bias_part[:, 2, :], bias_rest[:, 1, :]))
            step(nc.vector.tensor_scalar(bias_sel[:, 0, :], bias_part[:, 0, :], ident[0:3, 0:1], None, ALU.mult))
            for k in range(1, 3):
                step(nc.vector.scalar_tensor_tensor(bias_sel[:, k, :], bias_part[:, k, :], ident[0:3, k:k + 1],
                                                    bias_sel[:, k - 1, :], ALU.mult, ALU.add))
            nc.vector.tensor_copy(bias3[:, 0, :], bias_sel[:, 2, :])
            nc.vector.tensor_copy(bias3[:, 1, :], bias_sel[:, 2, :]).then_inc(bias_ready, 1)
            for g in range(1, SB):
                last = nc.vector.tensor_scalar(bucket_rows[:, SB_FIRST[g] - 1:SB_FIRST[g]],
                                               bucket_rows[:, SB_FIRST[g] - 1:SB_FIRST[g]], float(-GAP), None,
                                               ALU.add)
            step(last)
            step(nc.vector.tensor_reduce(most_rows[:, :], bucket_rows[:, :], AX_X, ALU.max))
            nc.vector.tensor_scalar(crowded[:, :], most_rows[:, :], float(WIN), None, ALU.is_gt)
            step(nc.vector.tensor_scalar(bucket_rows[:, :], bucket_rows[:, :], float(WIDE - 1), None, ALU.add))
            step(nc.vector.tensor_scalar(bucket_wins[:, :], bucket_rows[:, :], 6, None, ALU.logical_shift_right))
            step(nc.vector.tensor_scalar(bucket_wins_f[:, :], bucket_wins[:, :], 1.0, None, ALU.max))
            nc.vector.tensor_tensor_scan(win_ends[:, 1:BUCKETS + 1], zeros[0:1, 0:BUCKETS], bucket_wins_f[:, :], 0.0,
                                         ALU.add, ALU.add).then_inc(windows_ready, 1)

            for g in range(SB):
                first, end = superblock_quads(dve, g)
                with dve.Fori(first, end) as q:
                    dve.wait_ge(rank_used, q + 1)
                    for u in range(QUAD):
                        last = nc.vector.tensor_scalar(in_bucket[:, u, :],
                                                       iota_bucket[:, SB_FIRST[g]:SB_FIRST[g] + SB_NEXT],
                                                       bucket_slot[:, bass.ds(q * QUAD + u, 1)], None, ALU.is_equal)
                    last.then_inc(bucket_ready, 1)
                    for u in range(QUAD):
                        dve.wait_ge(scatter_done[u], q * 16 + 16)
                    nc.vector.tensor_copy(msg[:, :, D], src_slot[:, bass.ds(q * QUAD, QUAD)]).then_inc(src_put, 1)
                    dve.wait_ge(rank_psum, q + 1)
                    nc.vector.tensor_tensor(rank_prod[:, :, :], rank_bank[:, 0:QUAD * SB_NEXT].rearrange(
                        "p (u b) -> p u b", u=QUAD), in_bucket[:, :, :], ALU.mult).then_inc(rank_read, 1)
                    dve.wait_ge(rank_read, q + 1)
                    nc.vector.tensor_reduce(rank[:, :], rank_prod[:, :, :], AX_X, ALU.add).then_inc(rank_step, 1)
                    dve.wait_ge(rank_step, q + 1)
                    nc.vector.tensor_tensor(row_quad[:, :], rank[:, :], skip_slot[:, bass.ds(q * QUAD, QUAD)],
                                            ALU.add).then_inc(row_ready, 1)

            def put_rows(it, s, nodes):
                count = 2 if nodes == 2 * P else 1
                dve.wait_ge(win_in[s], it * 32 + 16 * count)
                for u in range(count):
                    last = nc.vector.tensor_scalar(place[:, s, u, :], iota_node[0:WIN, :], win_ring[:, s, u, D:D + 1],
                                                   neg_first[0:WIN, bass.ds((it * RING + s) * 2 + u, 1)],
                                                   ALU.subtract, ALU.is_equal)
                last.then_inc(place_ready, 1)

            def residual(it, s, nodes):
                count, rows = (2, P) if nodes == 2 * P else (1, nodes)
                dve.wait_ge(x_in[s], it * 16 + 16)
                dve.wait_ge(sum_psum, it * RING + s + 1)
                nc.vector.scalar_tensor_tensor(z_ring[0:rows, s, 0:count, :],
                                               sum_bank[SUM_BANK[s]][0:rows, 0:count * D].rearrange(
                                                   "p (u d) -> p u d", u=count), 0.0,
                                               x_ring[0:rows, s, 0:count, :], ALU.max, ALU.add).then_inc(z_ready, 1)

            def moments(it, s, nodes):
                count, rows = (2, P) if nodes == 2 * P else (1, nodes)
                dve.wait_ge(z_ready, it * RING + s + 1)
                for u in range(count):
                    last = nc.vector.bn_stats(stats[0:rows, s, u, :], z_ring[0:rows, s, u, :])
                last.then_inc(stats_ready, 1)

            def mean_and_var(it, s, nodes):
                count, rows = (2, P) if nodes == 2 * P else (1, nodes)
                dve.wait_ge(stats_ready, it * RING + s + 1)
                settle(dve)
                for u in range(count):
                    last = nc.vector.bn_aggr(mean_var[0:rows, s, u, :], stats[0:rows, s, u, :])
                last.then_inc(mv_ready, 1)

            def inverse(it, s):
                dve.wait_ge(std_ready, it * RING + s + 1)
                nc.vector.reciprocal(rstd[:, s, :], std[:, s, :]).then_inc(rstd_ready, 1)

            def shifts(it, s):
                dve.wait_ge(rstd_ready, it * RING + s + 1)
                nc.vector.scalar_tensor_tensor(shift[:, s, :], mean_var[:, s, :, 0], -1.0, rstd[:, s, :],
                                               ALU.mult, ALU.mult).then_inc(norm_ready, 1)

            def dve_step_of(it, s, fills, nodes):
                put_rows(it, s, nodes)
                if fills or s >= 1:
                    residual(*slot_before(it, s, 1), 2 * P)
                if fills or s >= 2:
                    inverse(*slot_before(it, s, 2))
                if fills or s >= 1:
                    moments(*slot_before(it, s, 1), 2 * P)
                if fills or s >= 2:
                    shifts(*slot_before(it, s, 2))
                if fills or s >= 1:
                    mean_and_var(*slot_before(it, s, 1), 2 * P)

            for s in range(RING):
                dve_step_of(0, s, False, 2 * P)
            with dve.Fori(1, ROUNDS - 1) as it:
                for s in range(RING):
                    dve_step_of(it, s, True, 2 * P)
            it = ROUNDS - 1
            for s in range(RING):
                dve_step_of(it, s, True, 2 * P if s < RING - 1 else LAST)
            residual(it, RING - 1, LAST)
            inverse(it, RING - 2)
            moments(it, RING - 1, LAST)
            shifts(it, RING - 2)
            mean_and_var(it, RING - 1, LAST)
            inverse(it, RING - 1)
            shifts(it, RING - 1)

            dve.sem_inc(z_again, 1)

            def again_steps(b, nodes, w0, w1):
                with dve.Fori(w0, w1) as w:
                    dve.wait_ge(rows_again, w * 16 + 16)
                    nc.vector.tensor_scalar(place[0:WIDE, 0, 0, :], iota_node[0:WIDE, :],
                                            win_ring[0:WIDE, 0, 0, D:D + 1], neg_first[0:WIDE, bass.ds(b, 1)],
                                            ALU.subtract, ALU.is_equal).then_inc(place_again, 1)
                dve.wait_ge(summed_again, w1 + 1)
                dve.wait_ge(x_again, b * 16 + 16)
                dve.wait_ge(y_again, b + 1)
                nc.vector.scalar_tensor_tensor(z_ring[0:nodes, 0, 0, :], sum_bank[0][0:nodes, 0:D], 0.0,
                                               x_ring[0:nodes, 0, 0, :], ALU.max, ALU.add).then_inc(z_again, 1)
                dve.wait_ge(z_again, b + 2)
                nc.vector.bn_stats(stats[0:nodes, 0, 0, :], z_ring[0:nodes, 0, 0, :]).then_inc(dve_again, 1)
                dve.wait_ge(dve_again, b * 2 + 1)
                settle(dve)
                nc.vector.bn_aggr(mean_var[0:nodes, 0, 0, :], stats[0:nodes, 0, 0, :]).then_inc(norm_again, 1)
                dve.wait_ge(std_again, b + 1)
                nc.vector.reciprocal(rstd[:, 0, 0:1], std[:, 0, 0:1]).then_inc(dve_again, 1)
                dve.wait_ge(dve_again, b * 2 + 2)
                nc.vector.scalar_tensor_tensor(shift[:, 0, 0:1], mean_var[:, 0, 0, 0:1], -1.0, rstd[:, 0, 0:1],
                                               ALU.mult, ALU.mult).then_inc(norm_again, 1)

            again(dve, again_steps)


def kernel(x, src, dst, edge_type_8, L0_gnn_weight, L0_gnn_bias):
    import numpy as _np
    import concourse.bacc as _bacc
    from concourse import mybir as _mybir
    from concourse.bass_utils import run_bass_kernel_spmd as _run

    nc = _bacc.Bacc("TRN2", target_bir_lowering=False, num_devices=1)
    arrays = {
        "x_dram": _np.ascontiguousarray(x),
        "src_dram": _np.ascontiguousarray(src).reshape(EP, EC),
        "dst_dram": _np.ascontiguousarray(dst).reshape(EP, EC),
        "type_dram": _np.ascontiguousarray(edge_type_8).reshape(EP, EC),
        "weight_dram": _np.ascontiguousarray(L0_gnn_weight),
        "bias_dram": _np.ascontiguousarray(L0_gnn_bias).reshape(1, D),
    }
    args = [nc.dram_tensor(k, a.shape, _mybir.dt.from_np(a.dtype), kind="ExternalInput").ap()
            for k, a in arrays.items()]
    out = nc.dram_tensor("out_dram", (N, D), F32, kind="ExternalOutput").ap()
    gnn_program(nc, *args, out)
    return _run(nc, [arrays], core_ids=[0]).results[0]["out_dram"]
```
